# Optimizing a Trainium2 kernel written in Bass

```python
import numpy as np
import jax
import jax.numpy as jnp

def _softmax(x, axis=-1):
    return jax.nn.softmax(x, axis=axis)
def _gelu(x):
    return jax.nn.gelu(x, approximate=True)
def _silu(x):
    return jax.nn.silu(x)
def _sigmoid(x):
    return jax.nn.sigmoid(x)
def _layernorm(x, axis=-1, eps=1e-5):
    m = jnp.mean(x, axis=axis, keepdims=True)
    v = jnp.var(x, axis=axis, keepdims=True)
    return (x - m) / jnp.sqrt(v + eps)
def _scatter_add(tgt, idx, src, axis=0):
    return tgt.at[idx].add(src)
def _segment_sum(src, seg, n):
    return jax.ops.segment_sum(src, seg, n)

kernel_name = 'mk_rec_standalone_d1_rec_860ceb'

def setup_inputs(seed: int = 0):
    np.random.seed(seed)
    _w = jnp.asarray
    def _rec_inputs():
        import jax
        import jax.numpy as jnp
        _rk = jax.random.key(seed)
        r_x = -0.000849101 + 1.0004 * jax.random.normal(jax.random.fold_in(_rk, 1), (1024, 39, 16), jnp.float32)
        return r_x
    r_x = _rec_inputs()
    def _L0_rec_setup():
        import jax, jax.numpy as jnp
        import numpy as np
        M_FIELDS = 39
        EMB_D = 16
        UNITS = [128, 128, 128]
        BATCH = 2048

        def _cin_forward(x, ws, bs):
            b, m, D = x.shape
            prev = x
            logit = []
            for k in range(len(ws)):
                h = prev.shape[1]
                z = jnp.einsum('bmd,bhd->bdmh', x, prev).reshape(b, D, m * h)
                t = jnp.einsum('bdc,co->bdo', z, ws[k]) + bs[k]
                t = jnp.transpose(t, (0, 2, 1))
                norm = jnp.sqrt(jnp.sum(t * t, axis=(-2, -1), keepdims=True))
                t = t / norm
                logit.append(t)
                prev = t
            return jnp.sum(jnp.concatenate(logit, axis=1), axis=-1)
        key = jax.random.key(seed)
        ks = jax.random.split(key, 4)
        x = jax.random.normal(ks[0], (BATCH, M_FIELDS, EMB_D), dtype=jnp.float32)
        w0 = jax.random.normal(ks[1], (M_FIELDS * M_FIELDS, UNITS[0]), dtype=jnp.float32) * 0.05
        w1 = jax.random.normal(ks[2], (UNITS[0] * M_FIELDS, UNITS[1]), dtype=jnp.float32) * 0.05
        w2 = jax.random.normal(ks[3], (UNITS[1] * M_FIELDS, UNITS[2]), dtype=jnp.float32) * 0.05
        b0 = jnp.zeros((UNITS[0],), dtype=jnp.float32)
        b1 = jnp.zeros((UNITS[1],), dtype=jnp.float32)
        b2 = jnp.zeros((UNITS[2],), dtype=jnp.float32)
        return {'x': x, 'w0': w0, 'w1': w1, 'w2': w2, 'b0': b0, 'b1': b1, 'b2': b2}
    _L0_rec_all = _L0_rec_setup()
    _L0_rec_in = {k: v for k, v in _L0_rec_all.items() if k in ('w0', 'w1', 'w2', 'b0', 'b1', 'b2', )}
    del _L0_rec_all

    return {
        "r_x": r_x,
        "L0_rec_w0": _L0_rec_in["w0"],
        "L0_rec_w1": _L0_rec_in["w1"],
        "L0_rec_w2": _L0_rec_in["w2"],
        "L0_rec_b0": _L0_rec_in["b0"],
        "L0_rec_b1": _L0_rec_in["b1"],
        "L0_rec_b2": _L0_rec_in["b2"],
    }

def reference(r_x, L0_rec_w0, L0_rec_w1, L0_rec_w2, L0_rec_b0, L0_rec_b1, L0_rec_b2):
    import jax
    import jax.numpy as jnp
    def _L0_rec_ref(x, w0, w1, w2, b0, b1, b2):
        import jax, jax.numpy as jnp
        import numpy as np
        M_FIELDS = 39
        EMB_D = 16
        UNITS = [128, 128, 128]
        BATCH = 2048

        def _cin_forward(x, ws, bs):
            b, m, D = x.shape
            prev = x
            logit = []
            for k in range(len(ws)):
                h = prev.shape[1]
                z = jnp.einsum('bmd,bhd->bdmh', x, prev).reshape(b, D, m * h)
                t = jnp.einsum('bdc,co->bdo', z, ws[k]) + bs[k]
                t = jnp.transpose(t, (0, 2, 1))
                norm = jnp.sqrt(jnp.sum(t * t, axis=(-2, -1), keepdims=True))
                t = t / norm
                logit.append(t)
                prev = t
            return jnp.sum(jnp.concatenate(logit, axis=1), axis=-1)
        return _cin_forward(x, [w0, w1, w2], [b0, b1, b2])

    y = _L0_rec_ref(r_x, L0_rec_w0, L0_rec_w1, L0_rec_w2, L0_rec_b0, L0_rec_b1, L0_rec_b2)
    return y


_drawn_inputs = setup_inputs


def setup_inputs(seed=0):
    import zlib

    import numpy as np

    out = dict(_drawn_inputs(seed))
    spreads = {'L0_rec_b0': (0.0, 0.1), 'L0_rec_b1': (0.0, 0.1), 'L0_rec_b2': (0.0, 0.1)}
    factors = {}
    for name, (base, spread) in spreads.items():
        noise = np.random.default_rng([zlib.crc32(name.encode()), seed]).standard_normal(out[name].shape)
        drawn = base * np.exp(spread * noise) if base else spread * noise
        out[name] = jnp.asarray(drawn.astype(out[name].dtype))
    for name, factor in factors.items():
        out[name] = (out[name] * factor).astype(out[name].dtype)
    return out
```

```python
import concourse.bass as bass
from concourse import mybir
from contextlib import ExitStack

FIELDS, COLS, UNITS, BATCH = 39, 16, 128, 1024
ROWS = 512
TILES = BATCH * COLS // ROWS
TB = ROWS // COLS
SHIFTS = FIELDS // 2 + 1
PER_K = 128 // FIELDS
K0 = -(-SHIFTS // PER_K)
LAST_K0 = (SHIFTS - PER_K * (K0 - 1)) * FIELDS

PATTERN = "PPFPDPFPPFPDPFPPFDPf"
GROUPS = len(PATTERN)
WIDTH = [1 if k == "f" else 2 for k in PATTERN]
KIND = [k.upper() for k in PATTERN]
FULL = sum(w for w, k in zip(WIDTH, KIND) if k == "F")
SPLIT = FIELDS - FULL
assert FULL + SPLIT == sum(WIDTH) == FIELDS


def first_field(g):
    full = KIND[g] == "F"
    before = sum(w for w, k in zip(WIDTH[:g], KIND[:g]) if (k == "F") == full)
    return before if full else FULL + before


FIELD = [first_field(g) for g in range(GROUPS)]
Z_SLOTS, ZH_SLOTS, ZL_SLOTS = 4, 3, 2
LOW_LAG = 1
DVE_LAG = 1
Z0_STEPS = [(0, 3, PER_K * FIELDS), (3, K0 - 1, PER_K * FIELDS), (K0 - 1, K0, LAST_K0)]
EVAC_AT, ROOT_AT, OUT_AT, PE_NORM_AT = 4, 5, 6, 1

STEPS = [(1, g) for g in range(GROUPS)] + [(2, g) for g in range(GROUPS)]
N = len(STEPS)


def order(kinds):
    out, n = [], 0
    for _, g in STEPS:
        out.append(n)
        n += KIND[g] in kinds
    return out, n


N_FULL, PER_FULL = order("F")
N_SPLIT, PER_SPLIT = order("PD")
N_POOL, PER_POOL = order("P")
N_DVE, PER_DVE = order("D")
assert KIND[GROUPS - 1] == "F" and KIND[GROUPS - 2] != "F" and LOW_LAG == 1
LAST_SPLIT = {1: GROUPS - 2, 2: 2 * GROUPS - 2}
SPLIT_STEPS = [s for s, (_, g) in enumerate(STEPS) if KIND[g] != "F"]


def cin(nc, x2, w0a, w0b, w1, w2, b0, b1, b2, out):
    f32, f32r = mybir.dt.float32, mybir.dt.float32r
    ALU, ACT, AX = mybir.AluOpType, mybir.ActivationFunctionType, mybir.AxisListType
    NROWS = TILES * ROWS

    with ExitStack() as ctx:
        def sb(name, shape, dt=f32):
            return ctx.enter_context(nc.sbuf_tensor(name, shape, dt))

        def bank(name, shape=(128, ROWS)):
            return ctx.enter_context(nc.psum_tensor(name, list(shape), f32))

        def sem(name):
            return ctx.enter_context(nc.semaphore(name))

        xb = sb("xb", [128, FIELDS, ROWS])
        z = sb("z", [128, Z_SLOTS, 2, ROWS])
        zh = sb("zh", [128, ZH_SLOTS, 2, ROWS], f32r)
        zl = sb("zl", [128, ZL_SLOTS, 2, ROWS], f32r)
        xa = sb("xa", [128, ROWS])
        x0 = sb("x0", [128, K0, ROWS])
        w0s = sb("w0s", [128, K0, UNITS])
        wf = sb("wf", [128, 2, FULL, UNITS])
        wh = sb("wh", [128, 2, SPLIT, UNITS], f32r)
        wl = sb("wl", [128, 2, SPLIT, UNITS], f32r)
        bias = sb("bias", [128, 3])
        ones = sb("ones", [128, 128])
        u = sb("u", [128, ROWS])
        ssq = sb("ssq", [128, TB])
        usum = sb("usum", [128, TB])
        root = sb("root", [128, TB])
        rroot = sb("rroot", [128, TB])
        quot = sb("quot", [128, TB])
        twice = sb("twice", [128, TB])
        rinv = sb("rinv", [128, TB])
        outb = sb("outb", [128, 3, TB])
        acc = [bank(f"acc{k}") for k in range(3)]
        prev = [bank(f"prev{k}") for k in range(2)]
        sq = bank("sq")
        nrm = bank("nrm", (128, TB))

        STAGED = 2 * SPLIT * UNITS // ROWS + 1
        STAGE_AT = FIELDS - STAGED
        staged = xb[:, STAGE_AT:, :].rearrange("p m r -> p (m r)")[:, 0:2 * SPLIT * UNITS].rearrange(
            "p (k m o) -> p k m o", k=2, o=UNITS)
        w0b_at = x0[:, 0:2, :].rearrange("p m r -> p (m r)")[:, 0:K0 * UNITS].rearrange("p (j o) -> p j o", o=UNITS)

        xb_loaded = [sem(f"xb_loaded{g}") for g in range(GROUPS)]
        x0_loaded = sem("x0_loaded")
        w0_loaded = sem("w0_loaded")
        wf_loaded = [sem("wf_loaded1"), sem("wf_loaded2")]
        ws_loaded = [sem("ws_loaded1"), sem("ws_loaded2")]
        bias_loaded = sem("bias_loaded")
        w0b_zeroed = sem("w0b_zeroed")
        ones_set = sem("ones_set")
        w0_summed = sem("w0_summed")
        wh_ready = sem("wh_ready")
        wl_ready = sem("wl_ready")
        z_ready = sem("z_ready")
        z0_ready = sem("z0_ready")
        zh_ready = sem("zh_ready")
        zl_pool = sem("zl_pool")
        zl_dve = sem("zl_dve")
        full_used = sem("full_used")
        zh_used = sem("zh_used")
        zl_used = sem("zl_used")
        acc0_ready = sem("acc0_ready")
        sq_ready = sem("sq_ready")
        u_ready = sem("u_ready")
        ssq_ready = sem("ssq_ready")
        usum_ready = sem("usum_ready")
        nrm_ready = sem("nrm_ready")
        root_ready = sem("root_ready")
        chain = sem("chain")
        prev_ready = [sem(f"prev_ready{k}") for k in range(2)]
        out_ready = sem("out_ready")
        out_stored = [sem(f"out_stored{k}") for k in range(3)]
        CHAIN = 4

        def wait(eng, s, value):
            if not isinstance(value, int) or value > 0:
                eng.wait_ge(s, value)

        assert N % Z_SLOTS == 0
        ZH_AT = [n % ZH_SLOTS for n in N_SPLIT]
        ZL_AT = [n % ZL_SLOTS for n in N_SPLIT]

        def split_user_before(step, at):
            n = N_SPLIT[step]
            for back in range(1, PER_SPLIT + 1):
                s = SPLIT_STEPS[(n - back) % PER_SPLIT]
                if at[s] == at[step]:
                    return s, -1 if n - back < 0 else 0

        def evac_no(layer, i):
            if layer == 0:
                return 0 if isinstance(i, int) and i == 0 else i * 3 - 1
            return i * 3 + (1 if layer == 1 else 3)

        def load_x0(sp, i):
            col = i * ROWS
            sp.dma_start(xa[0:PER_K * FIELDS, :],
                         bass.AP(x2.tensor, col, [[0, PER_K], [NROWS, FIELDS], [1, ROWS]])).then_inc(x0_loaded, 16)
            for r in range(PER_K):
                n = len(range(r, SHIFTS, PER_K))
                sp.dma_start(x0[r * FIELDS:(r + 1) * FIELDS, 0:n, :],
                             bass.AP(x2.tensor, r * NROWS + col,
                                     [[NROWS, FIELDS], [PER_K * NROWS, n], [1, ROWS]])).then_inc(x0_loaded, 16)

        X0_DMAS = (1 + PER_K) * 16

        def load_xb(sp, g, i):
            m, w = FIELD[g], WIDTH[g]
            sp.dma_start(xb[:, m:m + w, :],
                         bass.AP(x2.tensor, m * NROWS + i * ROWS, [[0, 128], [NROWS, w], [1, ROWS]])
                         ).then_inc(xb_loaded[g], 16)

        def store(sp, layer, i, e):
            sp.wait_ge(out_ready, e + 1)
            sp.dma_start(bass.AP(out.tensor, (i + layer * TILES) * (128 * TB), [[TB, 128], [1, TB]]),
                         outb[:, layer, :]).then_inc(out_stored[layer], 16)

        block = ctx.enter_context(nc.Block())

        @block.sync
        def _(sp):
            k3 = PER_K * (K0 - 1)
            sp.dma_start(w0s[0:PER_K * FIELDS, 0:K0 - 1, :],
                         w0a[0:k3].rearrange("(j r) h o -> (r h) j o", r=PER_K)).then_inc(w0_loaded, 16)
            sp.dma_start(w0s[0:LAST_K0, K0 - 1, :], w0a[k3:].rearrange("r h o -> (r h) o")).then_inc(w0_loaded, 16)
            sp.wait_ge(w0b_zeroed, 1)
            sp.dma_start(w0b_at[0:PER_K * FIELDS, 1:K0 - 1, :],
                         w0b[PER_K:k3].rearrange("(j r) h o -> (r h) j o", r=PER_K)).then_inc(w0_loaded, 16)
            sp.dma_start(w0b_at[0:LAST_K0, K0 - 1, :], w0b[k3:].rearrange("r h o -> (r h) o")).then_inc(w0_loaded, 16)
            sp.dma_start(w0b_at[FIELDS:PER_K * FIELDS, 0, :],
                         w0b[1:PER_K].rearrange("r h o -> (r h) o")).then_inc(w0_loaded, 16)
            for k, b in enumerate((b0, b1, b2)):
                sp.dma_start(bias[:, k:k + 1], b.rearrange("(o a) -> o a", a=1)).then_inc(bias_loaded, 16)
            sp.wait_ge(w0_summed, 2)
            load_x0(sp, 0)
            sp.dma_start(staged[:, 0, :, :], w1[:, FULL:, :]).then_inc(ws_loaded[0], 16)
            sp.dma_start(wf[:, 0, :, :], w1[:, 0:FULL, :]).then_inc(wf_loaded[0], 16)
            for g in range(GROUPS):
                if FIELD[g] + WIDTH[g] <= STAGE_AT:
                    load_xb(sp, g, 0)
            sp.dma_start(staged[:, 1, :, :], w2[:, FULL:, :]).then_inc(ws_loaded[1], 16)
            sp.dma_start(wf[:, 1, :, :], w2[:, 0:FULL, :]).then_inc(wf_loaded[1], 16)
            sp.wait_ge(wl_ready, 2)
            for g in range(GROUPS):
                if FIELD[g] + WIDTH[g] > STAGE_AT:
                    load_xb(sp, g, 0)

            def tile(i, first=False, last=False):
                if not last:
                    sp.wait_ge(acc0_ready, i + 1)
                    load_x0(sp, i + 1)
                if first:
                    store(sp, 0, 0, evac_no(0, 0))
                if not first:
                    store(sp, 2, i - 1, evac_no(2, i - 1))
                store(sp, 1, i, evac_no(1, i))
                if last:
                    store(sp, 2, i, evac_no(2, i) - 1)
                    return
                for g in range(GROUPS):
                    sp.wait_ge(z_ready, i * N + GROUPS + g + 1)
                    load_xb(sp, g, i + 1)
                    if g == GROUPS // 2 + 2:
                        store(sp, 0, i + 1, evac_no(0, i + 1))

            tile(0, first=True)
            with sp.Fori(1, TILES - 1) as i:
                tile(i)
            tile(TILES - 1, last=True)
            for k in range(3):
                sp.wait_ge(out_stored[k], 16 * TILES)

        @block.gpsimd
        def _(pool):
            nc.gpsimd.memset(ones[:], 1.0).then_inc(ones_set, 1)

            def low(s, i):
                wait(pool, zh_ready, i * PER_SPLIT + N_SPLIT[s] + 1)
                p, back = split_user_before(s, ZL_AT)
                wait(pool, zl_used, (i + back) * PER_SPLIT + N_SPLIT[p] + 1)
                w = WIDTH[STEPS[s][1]]
                nc.gpsimd.tensor_tensor(zl[:, ZL_AT[s], 0:w, :], z[:, s % Z_SLOTS, 0:w, :],
                                        zh[:, ZH_AT[s], 0:w, :].bitcast(f32), ALU.subtract).then_inc(zl_pool, 1)

            def tile(i):
                for s, (_, g) in enumerate(STEPS):
                    if KIND[g] == "P":
                        low(s, i)

            tile(0)
            with pool.Fori(1, TILES) as i:
                tile(i)

        @block.scalar
        def _(act):
            def high(s, i):
                act.wait_ge(z_ready, i * N + s + 1)
                p, back = split_user_before(s, ZH_AT)
                wait(act, zh_used, (i + back) * PER_SPLIT + N_SPLIT[p] + 1)
                if KIND[STEPS[p][1]] == "P":
                    wait(act, zl_pool, (i + back) * PER_POOL + N_POOL[p] + 1)
                else:
                    wait(act, zl_dve, (i + back) * PER_DVE + N_DVE[p] + 1)
                w = WIDTH[STEPS[s][1]]
                nc.scalar.activation(zh[:, ZH_AT[s], 0:w, :], z[:, s % Z_SLOTS, 0:w, :], ACT.Copy
                                     ).then_inc(zh_ready, 1)

            def evacuate(layer, i, e, last_prev0=None):
                if layer == 0:
                    act.wait_ge(acc0_ready, i + 1)
                else:
                    act.wait_ge(zl_used, i * PER_SPLIT + N_SPLIT[LAST_SPLIT[layer]] + 1)
                wait(act, ssq_ready, e)
                nc.scalar.activation(sq[:], acc[layer][:], ACT.Square, bias=bias[:, layer:layer + 1]
                                     ).then_inc(sq_ready, 1)
                wait(act, usum_ready, e)
                if layer == 2:
                    act.wait_ge(prev_ready[0], last_prev0)
                if layer == 0:
                    wait(act, prev_ready[1], i)
                nc.scalar.activation(u[:], acc[layer][:], ACT.Identity, bias=bias[:, layer:layer + 1]
                                     ).then_inc(u_ready, 1)

            def square_root(e):
                act.wait_ge(nrm_ready, e + 1)
                wait(act, chain, e * CHAIN)
                nc.scalar.activation(root[:], nrm[:], ACT.Sqrt).then_inc(root_ready, 1)

            act.wait_ge(bias_loaded, 48)
            for k in range(2):
                act.wait_ge(ws_loaded[k], 16)
                nc.scalar.activation(wh[:, k, :, :], staged[:, k, :, :], ACT.Copy).then_inc(wh_ready, 1)
                if k == 0:
                    evacuate(0, 0, 0)
                    square_root(0)

            def tile(i, first=False, last=False):
                for s, (layer, g) in enumerate(STEPS):
                    if layer == 1 and g == EVAC_AT and not first:
                        evacuate(2, i - 1, evac_no(2, i - 1), i + 1)
                    if layer == 1 and g == ROOT_AT and not first:
                        square_root(evac_no(2, i - 1))
                    if layer == 2 and g == 0:
                        evacuate(1, i, evac_no(1, i))
                        square_root(evac_no(1, i))
                    if layer == 2 and g == EVAC_AT and not last:
                        evacuate(0, i + 1, evac_no(0, i + 1))
                    if layer == 2 and g == ROOT_AT and not last:
                        square_root(evac_no(0, i + 1))
                    if KIND[g] != "F":
                        high(s, i)

            tile(0, first=True)
            with act.Fori(1, TILES - 1) as i:
                tile(i)
            tile(TILES - 1, last=True)
            evacuate(2, TILES - 1, evac_no(2, TILES - 1) - 1, TILES)
            square_root(evac_no(2, TILES - 1) - 1)

        @block.vector
        def _(dve):
            def product(s, i):
                layer, g = STEPS[s]
                if g == 0:
                    dve.wait_ge(prev_ready[layer - 1], i + 1)
                if layer == 1:
                    dve.wait_ge(xb_loaded[g], (i + 1) * 16)
                p, back = (s - Z_SLOTS) % N, (s - Z_SLOTS) // N
                kind = KIND[STEPS[p][1]]
                if kind == "F":
                    wait(dve, full_used, (i + back) * PER_FULL + N_FULL[p] + 1)
                elif kind == "P":
                    wait(dve, zl_pool, (i + back) * PER_POOL + N_POOL[p] + 1)
                else:
                    wait(dve, zl_dve, (i + back) * PER_DVE + N_DVE[p] + 1)
                m, w = FIELD[g], WIDTH[g]
                nc.vector.tensor_tensor(z[:, s % Z_SLOTS, 0:w, :],
                                        prev[layer - 1][:].unsqueeze(1).to_broadcast([128, w, ROWS]),
                                        xb[:, m:m + w, :], ALU.mult).then_inc(z_ready, 1)

            def low(s, i):
                dve.wait_ge(zh_ready, i * PER_SPLIT + N_SPLIT[s] + 1)
                p, back = split_user_before(s, ZL_AT)
                wait(dve, zl_used, (i + back) * PER_SPLIT + N_SPLIT[p] + 1)
                w = WIDTH[STEPS[s][1]]
                nc.vector.tensor_tensor(zl[:, ZL_AT[s], 0:w, :], z[:, s % Z_SLOTS, 0:w, :],
                                        zh[:, ZH_AT[s], 0:w, :].bitcast(f32), ALU.subtract).then_inc(zl_dve, 1)

            def products0(i):
                dve.wait_ge(x0_loaded, (i + 1) * X0_DMAS)
                for a, b, p in Z0_STEPS:
                    nc.vector.tensor_tensor(x0[0:p, a:b, :], x0[0:p, a:b, :],
                                            xa[0:p, :].unsqueeze(1).to_broadcast([p, b - a, ROWS]),
                                            ALU.mult).then_inc(z0_ready, 1)

            def square_sum(e):
                dve.wait_ge(sq_ready, e + 1)
                wait(dve, nrm_ready, e)
                nc.vector.tensor_reduce(ssq[:], sq[:].rearrange("p (b d) -> p b d", d=COLS), AX.X, ALU.add
                                        ).then_inc(ssq_ready, 1)

            def normalise(layer, e):
                dve.wait_ge(root_ready, e + 1)
                nc.vector.reciprocal(rroot[:], root[:]).then_inc(chain, 1)
                dve.wait_ge(chain, e * CHAIN + 1)
                nc.vector.tensor_tensor(quot[:], nrm[:], rroot[:], ALU.mult).then_inc(chain, 1)
                dve.wait_ge(chain, e * CHAIN + 2)
                nc.vector.tensor_tensor(twice[:], quot[:], root[:], ALU.add).then_inc(chain, 1)
                dve.wait_ge(chain, e * CHAIN + 3)
                wait(dve, out_ready, e)
                nc.vector.reciprocal(rinv[:], twice[:]).then_inc(chain, 1)
                dve.wait_ge(chain, e * CHAIN + 4)
                if layer < 2:
                    dve.wait_ge(u_ready, e + 1)
                    nc.vector.scalar_tensor_tensor(
                        prev[layer][:].rearrange("p (b d) -> p b d", d=COLS),
                        u[:].rearrange("p (b d) -> p b d", d=COLS), 2.0,
                        rinv[:].unsqueeze(2).to_broadcast([128, TB, COLS]), ALU.mult, ALU.mult
                    ).then_inc(prev_ready[layer], 1)

            def output(layer, i, e):
                dve.wait_ge(u_ready, e + 1)
                nc.vector.tensor_reduce(usum[:], u[:].rearrange("p (b d) -> p b d", d=COLS), AX.X, ALU.add
                                        ).then_inc(usum_ready, 1)
                dve.wait_ge(usum_ready, e + 1)
                wait(dve, out_stored[layer], i * 16)
                nc.vector.scalar_tensor_tensor(outb[:, layer, :], usum[:], 2.0, rinv[:], ALU.mult, ALU.mult
                                               ).then_inc(out_ready, 1)

            nc.vector.memset(w0b_at[0:FIELDS, 0, :], 0.0).then_inc(w0b_zeroed, 1)
            dve.wait_ge(w0_loaded, 80)
            p = PER_K * FIELDS
            nc.vector.tensor_tensor(w0s[0:p, 0:K0 - 1, :], w0s[0:p, 0:K0 - 1, :], w0b_at[0:p, 0:K0 - 1, :],
                                    ALU.add).then_inc(w0_summed, 1)
            nc.vector.tensor_tensor(w0s[0:LAST_K0, K0 - 1, :], w0s[0:LAST_K0, K0 - 1, :],
                                    w0b_at[0:LAST_K0, K0 - 1, :], ALU.add).then_inc(w0_summed, 1)
            products0(0)
            for k in range(2):
                dve.wait_ge(wh_ready, k + 1)
                nc.vector.tensor_tensor(wl[:, k, :, :], staged[:, k, :, :], wh[:, k, :, :].bitcast(f32),
                                        ALU.subtract).then_inc(wl_ready, 1)
                if k == 0:
                    square_sum(0)
                    normalise(0, 0)
                    output(0, 0, 0)

            def tile(i, first=False, last=False):
                late = []
                for s, (layer, g) in enumerate(STEPS):
                    if layer == 2 and g == 0:
                        for t in late:
                            low(t, i)
                        late = []
                        if not last:
                            products0(i + 1)
                        e = evac_no(1, i)
                        square_sum(e)
                        normalise(1, e)
                    product(s, i)
                    if layer == 2 and g == 1:
                        output(1, i, evac_no(1, i))
                    if late and s - late[0] >= DVE_LAG:
                        low(late.pop(0), i)
                    if KIND[g] == "D":
                        late.append(s)
                    if layer == 1 and not first:
                        e = evac_no(2, i - 1)
                        if g == EVAC_AT:
                            square_sum(e)
                        if g == ROOT_AT:
                            normalise(2, e)
                        if g == OUT_AT:
                            output(2, i - 1, e)
                    if layer == 2 and not last:
                        e = evac_no(0, i + 1)
                        if g == EVAC_AT:
                            square_sum(e)
                        if g == ROOT_AT:
                            normalise(0, e)
                        if g == OUT_AT:
                            output(0, i + 1, e)
                for t in late:
                    low(t, i)

            tile(0, first=True)
            with dve.Fori(1, TILES - 1) as i:
                tile(i)
            tile(TILES - 1, last=True)
            e = evac_no(2, TILES - 1) - 1
            square_sum(e)
            normalise(2, e)
            output(2, TILES - 1, e)

        @block.tensor
        def _(pe):
            def layer0(i, norm_after=None):
                if not isinstance(i, int) or i > 0:
                    pe.wait_ge(u_ready, evac_no(0, i - 1) + 1)
                for n, (a, b, p) in enumerate(Z0_STEPS):
                    pe.wait_ge(z0_ready, i * len(Z0_STEPS) + n + 1)
                    for j in range(a, b):
                        mm = nc.tensor.matmul(acc[0][:], w0s[0:p, j, :], x0[0:p, j, :],
                                              start=j == 0, stop=j == K0 - 1)
                    if norm_after is not None and n == 0:
                        feature_sum(norm_after)
                mm.then_inc(acc0_ready, 1)

            def feature_sum(e):
                pe.wait_ge(ssq_ready, e + 1)
                wait(pe, chain, e * CHAIN)
                nc.tensor.matmul(nrm[:], ones[:], ssq[:], start=True, stop=True).then_inc(nrm_ready, 1)

            def tile(i, first=False, last=False):
                for layer in (1, 2):
                    k = layer - 1
                    base = k * GROUPS
                    if layer == 2:
                        if last:
                            feature_sum(evac_no(1, i))
                        else:
                            layer0(i + 1, norm_after=evac_no(1, i))
                    passes = []
                    for g in range(GROUPS + LOW_LAG):
                        if g < GROUPS:
                            passes.append(("full" if KIND[g] == "F" else "high", g))
                        if g >= LOW_LAG and KIND[g - LOW_LAG] != "F":
                            passes.append(("low", g - LOW_LAG))
                    if not first:
                        pe.wait_ge(u_ready, evac_no(layer, i - 1) + 1)
                    for n, (what, g) in enumerate(passes):
                        s = base + g
                        m, w = FIELD[g], WIDTH[g]
                        start, stop = n == 0, n == len(passes) - 1
                        if what == "full":
                            if first:
                                pe.wait_ge(wf_loaded[k], 16)
                            pe.wait_ge(z_ready, i * N + s + 1)
                            for t in range(w):
                                mm = nc.tensor.matmul(acc[layer][:], wf[:, k, m + t, :], z[:, s % Z_SLOTS, t, :],
                                                      start=start and t == 0, stop=stop and t == w - 1)
                            mm.then_inc(full_used, 1)
                        elif what == "high":
                            if first and g == 0:
                                pe.wait_ge(wl_ready, layer)
                            pe.wait_ge(zh_ready, i * PER_SPLIT + N_SPLIT[s] + 1)
                            for t in range(w):
                                for part in (wh, wl):
                                    mm = nc.tensor.matmul(acc[layer][:], part[:, k, m - FULL + t, :],
                                                          zh[:, ZH_AT[s], t, :],
                                                          start=start and t == 0 and part is wh, stop=False)
                            mm.then_inc(zh_used, 1)
                        else:
                            if KIND[g] == "P":
                                pe.wait_ge(zl_pool, i * PER_POOL + N_POOL[s] + 1)
                            else:
                                pe.wait_ge(zl_dve, i * PER_DVE + N_DVE[s] + 1)
                            for t in range(w):
                                mm = nc.tensor.matmul(acc[layer][:], wh[:, k, m - FULL + t, :],
                                                      zl[:, ZL_AT[s], t, :], start=False, stop=stop and t == w - 1)
                            mm.then_inc(zl_used, 1)
                        if layer == 1 and g == PE_NORM_AT and not first and what != "low":
                            feature_sum(evac_no(2, i - 1))
                        if layer == 2 and g == PE_NORM_AT and not last and what != "low":
                            feature_sum(evac_no(0, i + 1))

            pe.wait_ge(ones_set, 1)
            pe.wait_ge(w0_summed, 2)
            layer0(0)
            feature_sum(0)
            tile(0, first=True)
            with pe.Fori(1, TILES - 1) as i:
                tile(i)
            tile(TILES - 1, last=True)
            feature_sum(evac_no(2, TILES - 1) - 1)


def kernel(r_x, L0_rec_w0, L0_rec_w1, L0_rec_w2, L0_rec_b0, L0_rec_b1, L0_rec_b2):
    import numpy as np
    import concourse.bacc as bacc
    from concourse.bass_utils import run_bass_kernel_spmd

    xt = np.asarray(r_x).transpose(1, 0, 2).reshape(FIELDS, BATCH * COLS)
    h = np.arange(FIELDS)[None, :]
    shifted = (h + np.arange(SHIFTS)[:, None]) % FIELDS
    w0 = np.asarray(L0_rec_w0).reshape(FIELDS, FIELDS, UNITS)
    arrays = {
        "x2": np.concatenate([xt, xt], axis=0),
        "w0a": w0[h, shifted],
        "w0b": w0[shifted, h],
        "w1": np.asarray(L0_rec_w1).reshape(FIELDS, UNITS, UNITS).transpose(1, 0, 2),
        "w2": np.asarray(L0_rec_w2).reshape(FIELDS, UNITS, UNITS).transpose(1, 0, 2),
        "b0": np.asarray(L0_rec_b0),
        "b1": np.asarray(L0_rec_b1),
        "b2": np.asarray(L0_rec_b2),
    }
    arrays = {k: np.ascontiguousarray(v) for k, v in arrays.items()}
    nc = bacc.Bacc("TRN2", target_bir_lowering=False, num_devices=1)
    args = [nc.dram_tensor(k, v.shape, mybir.dt.from_np(v.dtype), kind="ExternalInput").ap()
            for k, v in arrays.items()]
    out = nc.dram_tensor("out", (3, TILES, 128, TB), mybir.dt.float32, kind="ExternalOutput").ap()
    cin(nc, *args, out)
    r = run_bass_kernel_spmd(nc, [arrays], core_ids=[0])
    got = r.results[0]["out"]
    return got.transpose(1, 3, 0, 2).reshape(BATCH, 3 * UNITS)
```

```python
import concourse.bass as bass
from concourse import mybir
from contextlib import ExitStack

FIELDS, COLS, UNITS, BATCH = 39, 16, 128, 1024
ROWS = 512
TILES = BATCH * COLS // ROWS
TB = ROWS // COLS
SHIFTS = FIELDS // 2 + 1
PER_K = 128 // FIELDS
K0 = -(-SHIFTS // PER_K)
LAST_K0 = (SHIFTS - PER_K * (K0 - 1)) * FIELDS

PATTERN = "PFPDFPPPFDPPFPPDFPPf"
GROUPS = len(PATTERN)
WIDTH = [1 if k == "f" else 2 for k in PATTERN]
KIND = [k.upper() for k in PATTERN]
FULL = sum(w for w, k in zip(WIDTH, KIND) if k == "F")
SPLIT = FIELDS - FULL
assert FULL + SPLIT == sum(WIDTH) == FIELDS


def first_field(g):
    full = KIND[g] == "F"
    before = sum(w for w, k in zip(WIDTH[:g], KIND[:g]) if (k == "F") == full)
    return before if full else FULL + before


FIELD = [first_field(g) for g in range(GROUPS)]
ZF_SLOTS, ZS_SLOTS = 2, 4
ZH_SLOTS, ZL_SLOTS = 4, 4
LOW_LAG = 2
DVE_LAG = 2
W2_AT = 2
Z0_STEPS = [(0, 3, PER_K * FIELDS), (3, K0 - 1, PER_K * FIELDS), (K0 - 1, K0, LAST_K0)]
SCALE_AT = {2: 4}
U_AT = {2: 5, 1: 0, 0: 5}
SUM_AT = {2: 6, 1: 3, 0: 7}
FEATURES_AT = {2: 5, 1: 1, 0: 6}
ROOT_AT = {2: 9, 1: 5, 0: 10}
CHAIN_AT = {2: 10, 1: 6, 0: 11}

STEPS = [(1, g) for g in range(GROUPS)] + [(2, g) for g in range(GROUPS)]
N = len(STEPS)


def order(kinds, per_group=False):
    out, n = [], 0
    for _, g in STEPS:
        out.append(n)
        n += (KIND[g] in kinds) * (1 if per_group else WIDTH[g])
    return out, n


N_FULL, PER_FULL = order("F", per_group=True)
N_SPLITG, PER_SPLITG = order("PD", per_group=True)
N_SPLIT, PER_SPLIT = order("PD")
N_POOL, PER_POOL = order("P")
N_DVE, PER_DVE = order("D")
FULL_STEPS = [s for s, (_, g) in enumerate(STEPS) if KIND[g] == "F"]
SPLIT_STEPS = [s for s, (_, g) in enumerate(STEPS) if KIND[g] != "F"]
SPLIT_TILES = [(s, t) for s in SPLIT_STEPS for t in range(WIDTH[STEPS[s][1]])]


def user_before(n, per, slots):
    if n >= slots:
        return n - slots, 0
    return max(m for m in range(per) if m % slots == n % slots), -1


def passes(lag):
    tiles = [(g, t) for g in range(GROUPS) for t in range(WIDTH[g])]
    out = []
    for n in range(len(tiles) + lag):
        if n < len(tiles):
            g, t = tiles[n]
            out.append(("full" if KIND[g] == "F" else "high", g, t))
        if n >= lag:
            g, t = tiles[n - lag]
            if KIND[g] != "F":
                out.append(("low", g, t))
    return out


PASSES = passes(LOW_LAG)
assert PASSES[-1][0] == "low"
LAST_LOW = {1: N_SPLIT[GROUPS], 2: PER_SPLIT}


def cin(nc, x2, w0a, w0b, w1, w2, b0, b1, b2, out):
    f32, f32r = mybir.dt.float32, mybir.dt.float32r
    ALU, ACT, AX = mybir.AluOpType, mybir.ActivationFunctionType, mybir.AxisListType
    NROWS = TILES * ROWS

    with ExitStack() as ctx:
        def sb(name, shape, dt=f32):
            return ctx.enter_context(nc.sbuf_tensor(name, shape, dt))

        def bank(name, shape=(128, ROWS)):
            return ctx.enter_context(nc.psum_tensor(name, list(shape), f32))

        def sem(name):
            return ctx.enter_context(nc.semaphore(name))

        xb = sb("xb", [128, FIELDS, ROWS])
        zf = sb("zf", [128, ZF_SLOTS, 2, ROWS])
        zs = sb("zs", [128, ZS_SLOTS, 2, ROWS])
        zh = sb("zh", [128, ZH_SLOTS, ROWS], f32r)
        zl = sb("zl", [128, ZL_SLOTS, ROWS], f32r)
        xa = sb("xa", [128, ROWS])
        x0 = sb("x0", [128, K0, ROWS])
        w0s = sb("w0s", [128, K0, UNITS])
        wf = sb("wf", [128, 2, FULL, UNITS])
        wh = sb("wh", [128, 2, SPLIT, UNITS], f32r)
        wl = sb("wl", [128, 2, SPLIT, UNITS], f32r)
        bias = sb("bias", [128, 3])
        ones = sb("ones", [128, 128])
        ssq = sb("ssq", [128, TB])
        usum = sb("usum", [128, TB])
        root = sb("root", [128, TB])
        rroot = sb("rroot", [128, TB])
        quot = sb("quot", [128, TB])
        twice = sb("twice", [128, TB])
        rinv = [sb(f"rinv{k}", [128, TB]) for k in range(3)]
        outb = sb("outb", [128, 3, TB])
        acc = [bank(f"acc{k}") for k in range(3)]
        u = [bank(f"u{k}") for k in range(3)]
        sq = bank("sq")
        nrm = bank("nrm", (128, TB))

        PER_ROW = ROWS // UNITS
        STAGE2 = FIELDS - -(-SPLIT // PER_ROW)
        STAGE1 = STAGE2 - -(-SPLIT // PER_ROW)
        STAGE0 = STAGE1 - -(-K0 // PER_ROW)

        def staged(at, n):
            return xb[:, at:, :].rearrange("p m r -> p (m r)")[:, 0:n * UNITS].rearrange("p (m o) -> p m o", o=UNITS)

        w0b_at = staged(STAGE0, K0)
        ws_at = [staged(STAGE1, SPLIT), staged(STAGE2, SPLIT)]
        PARTS = [(n * SPLIT // 4, (n + 1) * SPLIT // 4) for n in range(4)]
        PART_OF = [n for n, (a, b) in enumerate(PARTS) for _ in range(a, b)]

        xb_loaded = [sem(f"xb_loaded{g}") for g in range(GROUPS)]
        x0_loaded = sem("x0_loaded")
        w0_loaded = sem("w0_loaded")
        wf_loaded = [sem("wf_loaded1"), sem("wf_loaded2")]
        ws_loaded = [[sem(f"ws_loaded{k}_{n}") for n in range(len(PARTS))] for k in (1, 2)]
        bias_loaded = sem("bias_loaded")
        w0b_zeroed = sem("w0b_zeroed")
        ones_set = sem("ones_set")
        w0_summed = sem("w0_summed")
        wh_ready = sem("wh_ready")
        wl_ready = sem("wl_ready")
        z_ready = sem("z_ready")
        z0_ready = sem("z0_ready")
        zh_ready = sem("zh_ready")
        zl_pool = sem("zl_pool")
        zl_dve = sem("zl_dve")
        full_used = sem("full_used")
        zh_used = sem("zh_used")
        zl_used = sem("zl_used")
        acc0_ready = sem("acc0_ready")
        sq_ready = sem("sq_ready")
        u_ready = [sem(f"u_ready{k}") for k in range(3)]
        ssq_ready = sem("ssq_ready")
        summed = [sem(f"summed{k}") for k in range(3)]
        nrm_ready = sem("nrm_ready")
        root_ready = sem("root_ready")
        chain = sem("chain")
        scaled_ready = sem("scaled_ready")
        out_ready = sem("out_ready")
        out_stored = [sem(f"out_stored{k}") for k in range(3)]
        CHAIN = 4

        def wait(eng, s, value):
            if not isinstance(value, int) or value > 0:
                eng.wait_ge(s, value)

        def zs_at(s):
            return zs[:, N_SPLITG[s] % ZS_SLOTS, :, :]

        def zh_at(s, t):
            return zh[:, (N_SPLIT[s] + t) % ZH_SLOTS, :]

        def zl_at(s, t):
            return zl[:, (N_SPLIT[s] + t) % ZL_SLOTS, :]

        def low_done(s, t, i):
            if KIND[STEPS[s][1]] == "P":
                return zl_pool, i * PER_POOL + N_POOL[s] + t + 1
            return zl_dve, i * PER_DVE + N_DVE[s] + t + 1

        def evac_no(layer, i):
            if layer == 0:
                return 0 if isinstance(i, int) and i == 0 else i * 3 - 1
            return i * 3 + (1 if layer == 1 else 3)

        def load_x0(sp, i):
            col = i * ROWS
            sp.dma_start(xa[0:PER_K * FIELDS, :],
                         bass.AP(x2.tensor, col, [[0, PER_K], [NROWS, FIELDS], [1, ROWS]])).then_inc(x0_loaded, 16)
            for r in range(PER_K):
                n = len(range(r, SHIFTS, PER_K))
                sp.dma_start(x0[r * FIELDS:(r + 1) * FIELDS, 0:n, :],
                             bass.AP(x2.tensor, r * NROWS + col,
                                     [[NROWS, FIELDS], [PER_K * NROWS, n], [1, ROWS]])).then_inc(x0_loaded, 16)

        X0_DMAS = (1 + PER_K) * 16

        def load_xb(sp, g, i):
            m, w = FIELD[g], WIDTH[g]
            sp.dma_start(xb[:, m:m + w, :],
                         bass.AP(x2.tensor, m * NROWS + i * ROWS, [[0, 128], [NROWS, w], [1, ROWS]])
                         ).then_inc(xb_loaded[g], 16)

        def store(sp, layer, i, e):
            sp.wait_ge(out_ready, e + 1)
            sp.dma_start(bass.AP(out.tensor, (i + layer * TILES) * (128 * TB), [[TB, 128], [1, TB]]),
                         outb[:, layer, :]).then_inc(out_stored[layer], 16)

        block = ctx.enter_context(nc.Block())

        LAST_EVAC = evac_no(2, TILES - 1) - 1

        def evacuations(layer, i, first, last):
            if layer == 1:
                return [(0, 0, 0, None)] if first else [(2, i - 1, evac_no(2, i - 1), i * 2)]
            found = [(1, i, evac_no(1, i), i * 2 + 1)]
            return found if last else found + [(0, i + 1, evac_no(0, i + 1), None)]

        @block.sync
        def _(sp):
            k3 = PER_K * (K0 - 1)
            sp.dma_start(w0s[0:PER_K * FIELDS, 0:K0 - 1, :],
                         w0a[0:k3].rearrange("(j r) h o -> (r h) j o", r=PER_K)).then_inc(w0_loaded, 16)
            sp.dma_start(w0s[0:LAST_K0, K0 - 1, :], w0a[k3:].rearrange("r h o -> (r h) o")).then_inc(w0_loaded, 16)
            sp.wait_ge(w0b_zeroed, 1)
            sp.dma_start(w0b_at[0:PER_K * FIELDS, 1:K0 - 1, :],
                         w0b[PER_K:k3].rearrange("(j r) h o -> (r h) j o", r=PER_K)).then_inc(w0_loaded, 16)
            sp.dma_start(w0b_at[0:LAST_K0, K0 - 1, :], w0b[k3:].rearrange("r h o -> (r h) o")).then_inc(w0_loaded, 16)
            sp.dma_start(w0b_at[FIELDS:PER_K * FIELDS, 0, :],
                         w0b[1:PER_K].rearrange("r h o -> (r h) o")).then_inc(w0_loaded, 16)
            for k, b in enumerate((b0, b1, b2)):
                sp.dma_start(bias[:, k:k + 1], b.rearrange("(o a) -> o a", a=1)).then_inc(bias_loaded, 16)
            load_x0(sp, 0)

            def load_weights(k, w):
                for n, (a, b) in enumerate(PARTS):
                    sp.dma_start(ws_at[k][:, a:b, :], w[:, FULL + a:FULL + b, :]).then_inc(ws_loaded[k][n], 16)
                sp.dma_start(wf[:, k, :, :], w[:, 0:FULL, :]).then_inc(wf_loaded[k], 16)

            load_weights(0, w1)
            for g in range(GROUPS):
                if g == 4:
                    load_weights(1, w2)
                end = FIELD[g] + WIDTH[g]
                if end > STAGE2:
                    sp.wait_ge(wl_ready, 2 * len(PARTS))
                elif end > STAGE0:
                    sp.wait_ge(w0_summed, 2)
                    sp.wait_ge(wl_ready, len(PARTS))
                load_xb(sp, g, 0)

            def tile(i, first=False, last=False):
                if not last:
                    sp.wait_ge(acc0_ready, i + 1)
                    load_x0(sp, i + 1)
                if first:
                    store(sp, 0, 0, evac_no(0, 0))
                if not first:
                    store(sp, 2, i - 1, evac_no(2, i - 1))
                store(sp, 1, i, evac_no(1, i))
                if last:
                    store(sp, 2, i, LAST_EVAC)
                    return
                for g in range(GROUPS):
                    sp.wait_ge(z_ready, i * N + GROUPS + g + 1)
                    load_xb(sp, g, i + 1)
                    if g == GROUPS // 2 + 2:
                        store(sp, 0, i + 1, evac_no(0, i + 1))

            tile(0, first=True)
            with sp.Fori(1, TILES - 1) as i:
                tile(i)
            tile(TILES - 1, last=True)
            for k in range(3):
                sp.wait_ge(out_stored[k], 16 * TILES)

        @block.gpsimd
        def _(pool):
            nc.gpsimd.memset(ones[:], 1.0).then_inc(ones_set, 1)

            def tile(i):
                for s, t in SPLIT_TILES:
                    if KIND[STEPS[s][1]] != "P":
                        continue
                    n = N_SPLIT[s] + t
                    wait(pool, zh_ready, i * PER_SPLIT + n + 1)
                    p, back = user_before(n, PER_SPLIT, ZL_SLOTS)
                    wait(pool, zl_used, (i + back) * PER_SPLIT + p + 1)
                    nc.gpsimd.tensor_tensor(zl_at(s, t), zs_at(s)[:, t, :], zh_at(s, t).bitcast(f32), ALU.subtract
                                            ).then_inc(zl_pool, 1)

            tile(0)
            with pool.Fori(1, TILES) as i:
                tile(i)

        @block.scalar
        def _(act):
            def high(s, i):
                act.wait_ge(z_ready, i * N + s + 1)
                for t in range(WIDTH[STEPS[s][1]]):
                    p, back = user_before(N_SPLIT[s] + t, PER_SPLIT, ZH_SLOTS)
                    wait(act, zh_used, (i + back) * PER_SPLIT + p + 1)
                    wait(act, *low_done(*SPLIT_TILES[p], i + back))
                    nc.scalar.activation(zh_at(s, t), zs_at(s)[:, t, :], ACT.Copy).then_inc(zh_ready, 1)

            def evacuate(layer, i, e, n_scaled=None):
                if layer == 0:
                    act.wait_ge(acc0_ready, i + 1)
                    wait(act, summed[0], i)
                    source = acc[0]
                else:
                    act.wait_ge(scaled_ready, n_scaled)
                    wait(act, summed[layer], i)
                    source = sq
                nc.scalar.activation(u[layer][:], source[:], ACT.Identity, bias=bias[:, layer:layer + 1]
                                     ).then_inc(u_ready[layer], 1)
                wait(act, ssq_ready, e)
                nc.scalar.activation(sq[:], source[:], ACT.Square, bias=bias[:, layer:layer + 1]
                                     ).then_inc(sq_ready, 1)

            def square_root(e):
                act.wait_ge(nrm_ready, e + 1)
                wait(act, chain, e * CHAIN)
                nc.scalar.activation(root[:], nrm[:], ACT.Sqrt).then_inc(root_ready, 1)

            act.wait_ge(bias_loaded, 48)
            def round_weights(k, n):
                act.wait_ge(ws_loaded[k][n], 16)
                a, b = PARTS[n]
                nc.scalar.activation(wh[:, k, a:b, :], ws_at[k][:, a:b, :], ACT.Copy).then_inc(wh_ready, 1)

            for n in range(len(PARTS)):
                round_weights(0, n)
            evacuate(0, 0, 0)

            def tile(i, first=False, last=False):
                for s, (layer, g) in enumerate(STEPS):
                    for k, j, e, n in evacuations(layer, i, first, last):
                        if g == U_AT[k] and not (first and layer == 1):
                            evacuate(k, j, e, n)
                        if g == ROOT_AT[k]:
                            square_root(e)
                    if KIND[g] != "F":
                        high(s, i)
                    if first and layer == 1 and 0 <= g - W2_AT < len(PARTS):
                        round_weights(1, g - W2_AT)

            tile(0, first=True)
            with act.Fori(1, TILES - 1) as i:
                tile(i)
            tile(TILES - 1, last=True)
            evacuate(2, TILES - 1, LAST_EVAC, 2 * TILES)
            square_root(LAST_EVAC)

        @block.vector
        def _(dve):
            def product(s, i):
                layer, g = STEPS[s]
                if g == 0:
                    dve.wait_ge(u_ready[layer - 1], i + 1)
                if layer == 1:
                    dve.wait_ge(xb_loaded[g], (i + 1) * 16)
                m, w = FIELD[g], WIDTH[g]
                if KIND[g] == "F":
                    n = N_FULL[s]
                    p, back = user_before(n, PER_FULL, ZF_SLOTS)
                    wait(dve, full_used, (i + back) * PER_FULL + p + 1)
                    z = zf[:, n % ZF_SLOTS, 0:w, :]
                else:
                    p, back = user_before(N_SPLITG[s], PER_SPLITG, ZS_SLOTS)
                    before = SPLIT_STEPS[p]
                    wait(dve, *low_done(before, WIDTH[STEPS[before][1]] - 1, i + back))
                    z = zs_at(s)[:, 0:w, :]
                nc.vector.tensor_tensor(z, u[layer - 1][:].unsqueeze(1).to_broadcast([128, w, ROWS]),
                                        xb[:, m:m + w, :], ALU.mult).then_inc(z_ready, 1)

            def low(s, i):
                for t in range(WIDTH[STEPS[s][1]]):
                    n = N_SPLIT[s] + t
                    dve.wait_ge(zh_ready, i * PER_SPLIT + n + 1)
                    p, back = user_before(n, PER_SPLIT, ZL_SLOTS)
                    wait(dve, zl_used, (i + back) * PER_SPLIT + p + 1)
                    nc.vector.tensor_tensor(zl_at(s, t), zs_at(s)[:, t, :], zh_at(s, t).bitcast(f32),
                                            ALU.subtract).then_inc(zl_dve, 1)

            def products0(i, n):
                dve.wait_ge(x0_loaded, (i + 1) * X0_DMAS)
                a, b, p = Z0_STEPS[n]
                nc.vector.tensor_tensor(x0[0:p, a:b, :], x0[0:p, a:b, :],
                                        xa[0:p, :].unsqueeze(1).to_broadcast([p, b - a, ROWS]),
                                        ALU.mult).then_inc(z0_ready, 1)

            def by_columns(ap):
                return ap.rearrange("p (b d) -> p b d", d=COLS)

            def scale(layer, i, before):
                dve.wait_ge(zl_used, i * PER_SPLIT + LAST_LOW[layer])
                wait(dve, ssq_ready, before)
                nc.vector.scalar_tensor_tensor(
                    by_columns(sq[:]), by_columns(acc[layer][:]), 2.0,
                    rinv[layer - 1][:].unsqueeze(2).to_broadcast([128, TB, COLS]), ALU.mult, ALU.mult
                ).then_inc(scaled_ready, 1)

            def square_sum(e):
                dve.wait_ge(sq_ready, e + 1)
                wait(dve, nrm_ready, e)
                nc.vector.tensor_reduce(ssq[:], by_columns(sq[:]), AX.X, ALU.add).then_inc(ssq_ready, 1)

            def norm_step(n, layer, e):
                if n == 0:
                    dve.wait_ge(root_ready, e + 1)
                else:
                    dve.wait_ge(chain, e * CHAIN + n)
                if n == 0:
                    ins = nc.vector.reciprocal(rroot[:], root[:])
                elif n == 1:
                    ins = nc.vector.tensor_tensor(quot[:], nrm[:], rroot[:], ALU.mult)
                elif n == 2:
                    ins = nc.vector.tensor_tensor(twice[:], quot[:], root[:], ALU.add)
                else:
                    ins = nc.vector.reciprocal(rinv[layer][:], twice[:])
                ins.then_inc(chain, 1)

            def column_sum(layer, i, e):
                dve.wait_ge(u_ready[layer], i + 1)
                nc.vector.tensor_reduce(usum[:], by_columns(u[layer][:]), AX.X, ALU.add).then_inc(summed[layer], 1)

            def output(layer, i, e):
                dve.wait_ge(chain, (e + 1) * CHAIN)
                dve.wait_ge(summed[layer], i + 1)
                wait(dve, out_stored[layer], i * 16)
                nc.vector.scalar_tensor_tensor(outb[:, layer, :], usum[:], 2.0, rinv[layer][:], ALU.mult, ALU.mult
                                               ).then_inc(out_ready, 1)

            def finish(layer, i, e):
                square_sum(e)
                for n in range(CHAIN):
                    norm_step(n, layer, e)
                column_sum(layer, i, e)
                output(layer, i, e)

            nc.vector.memset(w0b_at[0:FIELDS, 0, :], 0.0).then_inc(w0b_zeroed, 1)
            dve.wait_ge(w0_loaded, 80)
            p = PER_K * FIELDS
            nc.vector.tensor_tensor(w0s[0:p, 0:K0 - 1, :], w0s[0:p, 0:K0 - 1, :], w0b_at[0:p, 0:K0 - 1, :],
                                    ALU.add).then_inc(w0_summed, 1)
            nc.vector.tensor_tensor(w0s[0:LAST_K0, K0 - 1, :], w0s[0:LAST_K0, K0 - 1, :],
                                    w0b_at[0:LAST_K0, K0 - 1, :], ALU.add).then_inc(w0_summed, 1)
            for n in range(len(Z0_STEPS)):
                products0(0, n)
            def low_weights(k, n):
                dve.wait_ge(wh_ready, k * len(PARTS) + n + 1)
                a, b = PARTS[n]
                nc.vector.tensor_tensor(wl[:, k, a:b, :], ws_at[k][:, a:b, :], wh[:, k, a:b, :].bitcast(f32),
                                        ALU.subtract).then_inc(wl_ready, 1)

            for n in range(len(PARTS)):
                low_weights(0, n)

            def tile(i, first=False, last=False):
                late = []
                for s, (layer, g) in enumerate(STEPS):
                    if layer == 2 and g == 0:
                        for t in late:
                            low(t, i)
                        late = []
                        if not last:
                            for n in range(len(Z0_STEPS) - 1):
                                products0(i + 1, n)
                        scale(1, i, evac_no(1, i))
                        if not last:
                            products0(i + 1, len(Z0_STEPS) - 1)
                    product(s, i)
                    if first and layer == 1 and 0 <= g - W2_AT < len(PARTS):
                        low_weights(1, g - W2_AT)
                    if late and s - late[0] >= DVE_LAG:
                        low(late.pop(0), i)
                    if KIND[g] == "D":
                        late.append(s)
                    for k, j, e, n in evacuations(layer, i, first, last):
                        if g == SCALE_AT.get(k):
                            scale(2, j, e)
                        if g == SUM_AT[k]:
                            square_sum(e)
                        if 0 <= g - CHAIN_AT[k] < CHAIN:
                            norm_step(g - CHAIN_AT[k], k, e)
                        if g == CHAIN_AT[k] + CHAIN:
                            column_sum(k, j, e)
                        if g == CHAIN_AT[k] + CHAIN + 1:
                            output(k, j, e)
                for t in late:
                    low(t, i)

            tile(0, first=True)
            with dve.Fori(1, TILES - 1) as i:
                tile(i)
            tile(TILES - 1, last=True)
            scale(2, TILES - 1, LAST_EVAC)
            finish(2, TILES - 1, LAST_EVAC)

        @block.tensor
        def _(pe):
            def layer0(i):
                wait(pe, sq_ready, evac_no(0, i - 1) + 1 if not isinstance(i, int) or i > 0 else 0)
                for n, (a, b, p) in enumerate(Z0_STEPS):
                    pe.wait_ge(z0_ready, i * len(Z0_STEPS) + n + 1)
                    for j in range(a, b):
                        mm = nc.tensor.matmul(acc[0][:], w0s[0:p, j, :], x0[0:p, j, :],
                                              start=j == 0, stop=j == K0 - 1)
                mm.then_inc(acc0_ready, 1)

            def feature_sum(e):
                pe.wait_ge(ssq_ready, e + 1)
                wait(pe, chain, e * CHAIN)
                nc.tensor.matmul(nrm[:], ones[:], ssq[:], start=True, stop=True).then_inc(nrm_ready, 1)

            def tile(i, first=False, last=False):
                for layer in (1, 2):
                    k = layer - 1
                    base = k * GROUPS
                    if layer == 2 and not last:
                        layer0(i + 1)
                    if not first:
                        pe.wait_ge(scaled_ready, i * 2 + layer - 2)
                    for n, (what, g, t) in enumerate(PASSES):
                        s = base + g
                        m = FIELD[g] + t
                        ends = t == WIDTH[g] - 1
                        start, stop = n == 0, n == len(PASSES) - 1
                        if what == "full":
                            if first:
                                pe.wait_ge(wf_loaded[k], 16)
                            if t == 0:
                                pe.wait_ge(z_ready, i * N + s + 1)
                            mm = nc.tensor.matmul(acc[layer][:], wf[:, k, m, :], zf[:, N_FULL[s] % ZF_SLOTS, t, :],
                                                  start=start, stop=stop)
                            if ends:
                                mm.then_inc(full_used, 1)
                        elif what == "high":
                            if first:
                                pe.wait_ge(wl_ready, k * len(PARTS) + PART_OF[m - FULL] + 1)
                            pe.wait_ge(zh_ready, i * PER_SPLIT + N_SPLIT[s] + t + 1)
                            nc.tensor.matmul(acc[layer][:], wh[:, k, m - FULL, :], zh_at(s, t),
                                             start=start, stop=False)
                            nc.tensor.matmul(acc[layer][:], wl[:, k, m - FULL, :], zh_at(s, t),
                                             start=False, stop=False).then_inc(zh_used, 1)
                        else:
                            pe.wait_ge(*low_done(s, t, i))
                            nc.tensor.matmul(acc[layer][:], wh[:, k, m - FULL, :], zl_at(s, t),
                                             start=False, stop=stop).then_inc(zl_used, 1)
                        if what != "low" and ends:
                            for j, _, e, _ in evacuations(layer, i, first, last):
                                if g == FEATURES_AT[j]:
                                    feature_sum(e)

            pe.wait_ge(ones_set, 1)
            pe.wait_ge(w0_summed, 2)
            layer0(0)
            tile(0, first=True)
            with pe.Fori(1, TILES - 1) as i:
                tile(i)
            tile(TILES - 1, last=True)
            feature_sum(LAST_EVAC)


def kernel(r_x, L0_rec_w0, L0_rec_w1, L0_rec_w2, L0_rec_b0, L0_rec_b1, L0_rec_b2):
    import numpy as np
    import concourse.bacc as bacc
    from concourse.bass_utils import run_bass_kernel_spmd

    xt = np.asarray(r_x).transpose(1, 0, 2).reshape(FIELDS, BATCH * COLS)
    h = np.arange(FIELDS)[None, :]
    shifted = (h + np.arange(SHIFTS)[:, None]) % FIELDS
    w0 = np.asarray(L0_rec_w0).reshape(FIELDS, FIELDS, UNITS)
    arrays = {
        "x2": np.concatenate([xt, xt], axis=0),
        "w0a": w0[h, shifted],
        "w0b": w0[shifted, h],
        "w1": np.asarray(L0_rec_w1).reshape(FIELDS, UNITS, UNITS).transpose(1, 0, 2),
        "w2": np.asarray(L0_rec_w2).reshape(FIELDS, UNITS, UNITS).transpose(1, 0, 2),
        "b0": np.asarray(L0_rec_b0),
        "b1": np.asarray(L0_rec_b1),
        "b2": np.asarray(L0_rec_b2),
    }
    arrays = {k: np.ascontiguousarray(v) for k, v in arrays.items()}
    nc = bacc.Bacc("TRN2", target_bir_lowering=False, num_devices=1)
    args = [nc.dram_tensor(k, v.shape, mybir.dt.from_np(v.dtype), kind="ExternalInput").ap()
            for k, v in arrays.items()]
    out = nc.dram_tensor("out", (3, TILES, 128, TB), mybir.dt.float32, kind="ExternalOutput").ap()
    cin(nc, *args, out)
    r = run_bass_kernel_spmd(nc, [arrays], core_ids=[0])
    got = r.results[0]["out"]
    return got.transpose(1, 3, 0, 2).reshape(BATCH, 3 * UNITS)
```

```python
import concourse.bass as bass
from concourse import mybir
from contextlib import ExitStack

FIELDS, COLS, UNITS, BATCH = 39, 16, 128, 1024
ROWS = 512
TILES = BATCH * COLS // ROWS
TB = ROWS // COLS
CHUNKS = ROWS // 128
PAIR = 2 * 128
SHIFTS = FIELDS // 2 + 1
PER_K = 128 // FIELDS
K0 = -(-SHIFTS // PER_K)
LAST_K0 = (SHIFTS - PER_K * (K0 - 1)) * FIELDS
K0_PARTS = [PER_K * FIELDS] * (K0 - 1) + [LAST_K0]

GROUP = ROWS // UNITS
GROUPS = -(-FIELDS // GROUP)
WIDTH = [min(GROUP, FIELDS - GROUP * g) for g in range(GROUPS)]
assert GROUP == 4
ODD_SLOTS = 2
EVEN_SLOTS = 3
EVEN_SLOT = [n % EVEN_SLOTS for n in range(4 * GROUPS)]
if EVEN_SLOT[-1] == 0:
    EVEN_SLOT[-1] = 1
PAIRS = 4
MACS = PAIRS * FIELDS
ADDS = GROUPS
PRODUCT_SLOTS = 8
assert GROUPS % ODD_SLOTS == 0 and PAIRS * GROUPS % PRODUCT_SLOTS == 0

TURN_AT = 4
LAYER0_AT = [6, 9, 11, 14, 15, 17, 19]
FEATURES_AT = {2: 8, 0: 21, 1: 29}
SQUARE2_AT, LAYER1_AT, SQUARE0_AT, SQUARE1_AT, HIGH0_AT = 6, {14: 0, 25: 1}, 20, 27, 30
ROOT_AT = {2: 10, 0: 22, 1: 29}
Z0_DVE_AT = {7: 0, 24: 1, 34: 2, 48: 3}
SCALE_AT = 18
LOW1_AT = {57: 0, 99: 1}
SUM_AT = {2: 27, 0: 78, 1: 108}
CHAIN_AT = {2: 39, 0: 89, 1: 116}
COLUMNS_AT = {2: 32, 0: 108, 1: 118}
OUTPUT_AT = {2: 51, 1: 126}
DIVIDE_AT = 97
LOW0_AT = 124
ROUND2_AT = [2, 4, 6, 8, 10]
LOW2_AT = [14, 22, 28, 38, 66]
Z0_POOL_AT = {4: 4, 6: 5, 9: 6}
assert sorted([*Z0_DVE_AT.values(), *Z0_POOL_AT.values()]) == list(range(K0))
N_Z0 = (len(Z0_DVE_AT), len(Z0_POOL_AT))


def cin(nc, x2, xr, eye, w0a, w0b, w1, w2, b0, b1, b2, out):
    f32, f32r = mybir.dt.float32, mybir.dt.float32r
    ALU, ACT, AX = mybir.AluOpType, mybir.ActivationFunctionType, mybir.AxisListType
    NROWS = TILES * ROWS
    DVE, POOL = 0, 1

    with ExitStack() as ctx:
        def sb(name, shape, dt=f32):
            return ctx.enter_context(nc.sbuf_tensor(name, shape, dt))

        def bank(name, shape=(128, ROWS)):
            return ctx.enter_context(nc.psum_tensor(name, list(shape), f32))

        def sem(name):
            return ctx.enter_context(nc.semaphore(name))

        xrow = [sb(f"xrow{k}", [128, CHUNKS, FIELDS]) for k in (1, 2)]
        ph = [sb(f"ph{k}", [128, ROWS], f32r) for k in (0, 1)]
        pl = [sb(f"pl{k}", [128, ROWS], f32r) for k in (0, 1)]
        products = sb("products", [128, PRODUCT_SLOTS, ROWS])
        prev0 = sb("prev0", [128, ROWS])
        u1 = sb("u1", [128, ROWS])
        u2 = sb("u2", [128, ROWS])
        sq = sb("sq", [128, ROWS])
        part = sb("part", [128, 2, UNITS])
        wide = sb("wide", [128, 2, ROWS])
        total = [sb(f"total{e}", [128, UNITS]) for e in (DVE, POOL)]
        identity = sb("identity", [128, 128])
        xa = sb("xa", [128, ROWS])
        x0 = sb("x0", [128, K0, ROWS])
        w0s = sb("w0s", [128, K0, UNITS])
        w0t = sb("w0t", [128, K0, UNITS])
        ws = sb("ws", [128, 2, FIELDS, UNITS])
        wh = sb("wh", [128, 2, FIELDS, UNITS], f32r)
        wl = sb("wl", [128, 2, FIELDS, UNITS], f32r)
        bias = sb("bias", [128, 3])
        ones = sb("ones", [128, 128])
        ssq = sb("ssq", [128, TB])
        usum = sb("usum", [128, TB])
        root = sb("root", [128, TB])
        rroot = sb("rroot", [128, TB])
        quot = sb("quot", [128, TB])
        half = sb("half", [128, TB])
        rinv = [sb(f"rinv{k}", [128, TB]) for k in range(3)]
        outb = sb("outb", [128, 3, TB])
        inner = [[bank(f"inner{e}_{n}") for n in range((EVEN_SLOTS, ODD_SLOTS)[e])] for e in (DVE, POOL)]
        acc0 = bank("acc0")
        acc12 = bank("acc12")
        nrm = bank("nrm", (128, TB))

        PARTS = [(n * FIELDS // len(ROUND2_AT), (n + 1) * FIELDS // len(ROUND2_AT)) for n in range(len(ROUND2_AT))]
        PART_OF = [n for n, (a, b) in enumerate(PARTS) for _ in range(a, b)]

        x0_loaded = sem("x0_loaded")
        xrow_loaded = [sem("xrow_loaded1"), sem("xrow_loaded2")]
        w0_loaded = sem("w0_loaded")
        ws_loaded = [[sem(f"ws_loaded{k}_{n}") for n in range(len(PARTS))] for k in (1, 2)]
        bias_loaded = sem("bias_loaded")
        identity_loaded = sem("identity_loaded")
        w0t_zeroed = sem("w0t_zeroed")
        ones_set = sem("ones_set")
        w0_summed = sem("w0_summed")
        wh_ready = sem("wh_ready")
        wl_ready = sem("wl_ready")
        z0_ready = [sem("z0_dve"), sem("z0_pool")]
        inner_ready = [sem("inner_dve"), sem("inner_pool")]
        macs = sem("macs")
        products_ready = sem("products_ready")
        adds = sem("adds")
        total_ready = [sem("total_dve"), sem("total_pool")]
        turned = sem("turned")
        acc0_ready = sem("acc0_ready")
        sq_ready = sem("sq_ready")
        u1_ready = sem("u1_ready")
        u2_ready = sem("u2_ready")
        prev0_ready = sem("prev0_ready")
        ph_ready = [sem("ph0_ready"), sem("ph1_ready")]
        pl_ready = [sem("pl0_ready"), sem("pl1_ready")]
        ssq_ready = sem("ssq_ready")
        summed = [None, sem("summed1"), sem("summed2")]
        nrm_ready = sem("nrm_ready")
        root_ready = sem("root_ready")
        chain = sem("chain")
        scaled_ready = sem("scaled_ready")
        out_ready = sem("out_ready")
        out_stored = [sem(f"out_stored{k}") for k in range(3)]
        CHAIN = 4

        def wait(eng, s, value):
            if not isinstance(value, int) or value > 0:
                eng.wait_ge(s, value)

        def evac_no(layer, i, last=False):
            if layer == 0:
                return 0 if isinstance(i, int) and i == 0 else i * 3 - 2
            return i * 3 + layer + 1 - last

        def mac_no(i, v, m):
            return i * MACS + v * FIELDS + m

        def macs_by(i, n):
            v, g = divmod(n, GROUPS)
            return mac_no(i, v, min((g + 1) * GROUP, FIELDS))

        def load_x0(sp, i):
            col = i * ROWS
            sp.dma_start(xa[0:PER_K * FIELDS, :],
                         bass.AP(x2.tensor, col, [[0, PER_K], [NROWS, FIELDS], [1, ROWS]])).then_inc(x0_loaded, 16)
            for r in range(PER_K):
                n = len(range(r, SHIFTS, PER_K))
                sp.dma_start(x0[r * FIELDS:(r + 1) * FIELDS, 0:n, :],
                             bass.AP(x2.tensor, r * NROWS + col,
                                     [[NROWS, FIELDS], [PER_K * NROWS, n], [1, ROWS]])).then_inc(x0_loaded, 16)

        X0_DMAS = (1 + PER_K) * 16

        def load_xrow(sp, k, i):
            n = CHUNKS * FIELDS
            sp.dma_start(xrow[k][:].rearrange("p c m -> p (c m)"),
                         bass.AP(xr.tensor, i * (128 * n), [[n, 128], [1, n]])).then_inc(xrow_loaded[k], 16)

        def store(sp, layer, i, e):
            sp.wait_ge(out_ready, e + 1)
            sp.dma_start(bass.AP(out.tensor, (i + layer * TILES) * (128 * TB), [[TB, 128], [1, TB]]),
                         outb[:, layer, :]).then_inc(out_stored[layer], 16)

        block = ctx.enter_context(nc.Block())

        @block.sync
        def _(sp):
            k3 = PER_K * (K0 - 1)
            sp.dma_start(w0s[0:PER_K * FIELDS, 0:K0 - 1, :],
                         w0a[0:k3].rearrange("(j r) h o -> (r h) j o", r=PER_K)).then_inc(w0_loaded, 16)
            sp.dma_start(w0s[0:LAST_K0, K0 - 1, :], w0a[k3:].rearrange("r h o -> (r h) o")).then_inc(w0_loaded, 16)
            sp.wait_ge(w0t_zeroed, 1)
            sp.dma_start(w0t[0:PER_K * FIELDS, 1:K0 - 1, :],
                         w0b[PER_K:k3].rearrange("(j r) h o -> (r h) j o", r=PER_K)).then_inc(w0_loaded, 16)
            sp.dma_start(w0t[0:LAST_K0, K0 - 1, :], w0b[k3:].rearrange("r h o -> (r h) o")).then_inc(w0_loaded, 16)
            sp.dma_start(w0t[FIELDS:PER_K * FIELDS, 0, :],
                         w0b[1:PER_K].rearrange("r h o -> (r h) o")).then_inc(w0_loaded, 16)
            load_x0(sp, 0)
            for k, b in enumerate((b0, b1, b2)):
                sp.dma_start(bias[:, k:k + 1], b.rearrange("(o a) -> o a", a=1)).then_inc(bias_loaded, 16)

            def load_weights(k, w):
                for n, (a, b) in enumerate(PARTS):
                    sp.dma_start(ws[:, k, a:b, :], w[:, a:b, :]).then_inc(ws_loaded[k][n], 16)

            load_weights(0, w1)
            load_xrow(sp, 0, 0)
            sp.dma_start(identity[:], eye).then_inc(identity_loaded, 16)
            load_weights(1, w2)

            def tile(i, first=False, last=False):
                if first:
                    store(sp, 0, 0, 0)
                if not last:
                    sp.wait_ge(acc0_ready, i + 1)
                    load_x0(sp, i + 1)
                if not first:
                    sp.wait_ge(macs, i * MACS)
                    sp.wait_ge(products_ready, i * PAIRS * GROUPS)
                load_xrow(sp, 1, i)
                if not first:
                    store(sp, 2, i - 1, evac_no(2, i - 1))
                if not last:
                    sp.wait_ge(macs, mac_no(i, 2, 0))
                    sp.wait_ge(products_ready, (i * PAIRS + 2) * GROUPS)
                    load_xrow(sp, 0, i + 1)
                    store(sp, 0, i + 1, evac_no(0, i + 1))
                store(sp, 1, i, evac_no(1, i, last))
                if last:
                    store(sp, 2, i, evac_no(2, i, last))

            tile(0, first=True)
            with sp.Fori(1, TILES - 1) as i:
                tile(i)
            tile(TILES - 1, last=True)
            for k in range(3):
                sp.wait_ge(out_stored[k], 16 * TILES)

        def product0(ops, e, j):
            p = K0_PARTS[j]
            ops.tensor_tensor(x0[0:p, j, :], x0[0:p, j, :], xa[0:p, :], ALU.mult).then_inc(z0_ready[e], 1)

        @block.gpsimd
        def _(pool):
            nc.gpsimd.memset(ones[:], 1.0).then_inc(ones_set, 1)
            pool.wait_ge(x0_loaded, X0_DMAS)
            for j in Z0_POOL_AT.values():
                product0(nc.gpsimd, POOL, j)

            def add_group(i, v, g):
                pair = i * PAIRS + v
                pool.wait_ge(products_ready, pair * GROUPS + g + 1)
                cols = slice(0, WIDTH[g] * UNITS)
                sum_ = wide[:, g % 2, cols]
                if g < 4:
                    wait(pool, total_ready[POOL], pair)
                    before = products[:, (v * GROUPS + g - 2) % PRODUCT_SLOTS, cols]
                else:
                    pool.wait_ge(adds, pair * ADDS + g - 3)
                    before = sum_
                nc.gpsimd.tensor_tensor(sum_, before, products[:, (v * GROUPS + g) % PRODUCT_SLOTS, cols], ALU.add
                                        ).then_inc(adds, 1)

            def merge(i, v):
                pair = i * PAIRS + v
                pool.wait_ge(adds, pair * ADDS + GROUPS - 2)
                nc.gpsimd.tensor_tensor(wide[:, 0, :], wide[:, 0, :], wide[:, 1, :], ALU.add).then_inc(adds, 1)
                h = ROWS // 2
                pool.wait_ge(adds, pair * ADDS + GROUPS - 1)
                nc.gpsimd.tensor_tensor(wide[:, 0, 0:h], wide[:, 0, 0:h], wide[:, 0, h:], ALU.add).then_inc(adds, 1)
                pool.wait_ge(adds, pair * ADDS + GROUPS)
                wait(pool, turned, pair)
                nc.gpsimd.tensor_tensor(total[POOL][:], wide[:, 0, 0:UNITS], wide[:, 0, UNITS:h], ALU.add
                                        ).then_inc(total_ready[POOL], 1)

            def tile(i, last=False):
                for v in range(PAIRS):
                    for g in range(2, GROUPS):
                        add_group(i, v, g)
                        if v == 0 and g in Z0_POOL_AT and not last:
                            pool.wait_ge(x0_loaded, (i + 2) * X0_DMAS)
                            product0(nc.gpsimd, POOL, Z0_POOL_AT[g])
                    merge(i, v)

            tile(0)
            with pool.Fori(1, TILES - 1) as i:
                tile(i)
            tile(TILES - 1, last=True)

        @block.scalar
        def _(act):
            def square0(i, e):
                act.wait_ge(acc0_ready, i + 1)
                wait(act, ssq_ready, e)
                nc.scalar.activation(sq[:], acc0[:], ACT.Square, bias=bias[:, 0:1]).then_inc(sq_ready, 1)

            def layer1(i, h):
                cols = slice(h * PAIR, (h + 1) * PAIR)
                act.wait_ge(turned, i * PAIRS + h + 1)
                wait(act, summed[1], i)
                wait(act, pl_ready[1], i * 2 + h - 1)
                wait(act, sq_ready, evac_no(1, i - 1) + 1 if not isinstance(i, int) or i > 0 else 0)
                nc.scalar.activation(u1[:, cols], acc12[:, cols], ACT.Identity, bias=bias[:, 1:2]
                                     ).then_inc(u1_ready, 1)
                nc.scalar.activation(ph[1][:, cols], acc12[:, cols], ACT.Identity, bias=bias[:, 1:2]
                                     ).then_inc(ph_ready[1], 1)

            def square1(i, e):
                act.wait_ge(u1_ready, i * 2 + 2)
                wait(act, ssq_ready, e)
                nc.scalar.activation(sq[:], u1[:], ACT.Square).then_inc(sq_ready, 1)

            def square2(i, e):
                act.wait_ge(scaled_ready, i + 1)
                wait(act, summed[2], i)
                nc.scalar.activation(u2[:], sq[:], ACT.Identity, bias=bias[:, 2:3]).then_inc(u2_ready, 1)
                nc.scalar.activation(sq[:], sq[:], ACT.Square, bias=bias[:, 2:3]).then_inc(sq_ready, 1)

            def square_root(e):
                act.wait_ge(nrm_ready, e + 1)
                wait(act, chain, e * CHAIN)
                nc.scalar.activation(root[:], nrm[:], ACT.Sqrt).then_inc(root_ready, 1)

            def high0(i):
                act.wait_ge(prev0_ready, i + 1)
                nc.scalar.activation(ph[0][:], prev0[:], ACT.Copy).then_inc(ph_ready[0], 1)

            def multiply(i, n):
                v, g = divmod(n, GROUPS)
                layer, h = 1 + v // 2, v % 2
                act.wait_ge(inner_ready[POOL], i * PAIRS * GROUPS + n + 1)
                if g == h == 0:
                    act.wait_ge(xrow_loaded[layer - 1], (i + 1) * 16)
                pv, pg = divmod(n - PRODUCT_SLOTS, GROUPS)
                wait(act, adds, (i * PAIRS + pv) * ADDS + (pg if pg < 2 else pg - 2) + 1)
                for t in range(WIDTH[g]):
                    cols = slice(t * UNITS, (t + 1) * UNITS)
                    m = g * GROUP + t
                    ins = nc.scalar.activation(products[:, n % PRODUCT_SLOTS, cols], inner[POOL][n % ODD_SLOTS][:, cols],
                                               ACT.Copy, scale=xrow[layer - 1][:, 2 * h + 1, m:m + 1])
                ins.then_inc(products_ready, 1)

            def round_weights(k, n):
                act.wait_ge(ws_loaded[k][n], 16)
                a, b = PARTS[n]
                nc.scalar.activation(wh[:, k, a:b, :], ws[:, k, a:b, :], ACT.Copy).then_inc(wh_ready, 1)

            act.wait_ge(bias_loaded, 48)
            for n in range(len(PARTS)):
                round_weights(0, n)
            square0(0, 0)
            square_root(0)
            high0(0)

            def tile(i, first=False, last=False):
                for n in range(PAIRS * GROUPS):
                    if n in LAYER1_AT:
                        layer1(i, LAYER1_AT[n])
                    if not first:
                        if n == SQUARE2_AT:
                            square2(i - 1, evac_no(2, i - 1))
                        if n == ROOT_AT[2]:
                            square_root(evac_no(2, i - 1))
                    if not last:
                        if n == SQUARE0_AT:
                            square0(i + 1, evac_no(0, i + 1))
                        if n == ROOT_AT[0]:
                            square_root(evac_no(0, i + 1))
                        if n == HIGH0_AT:
                            high0(i + 1)
                    if n == SQUARE1_AT:
                        square1(i, evac_no(1, i, last))
                    if n == ROOT_AT[1]:
                        square_root(evac_no(1, i, last))
                    if first and n in ROUND2_AT:
                        round_weights(1, ROUND2_AT.index(n))
                    multiply(i, n)

            tile(0, first=True)
            with act.Fori(1, TILES - 1) as i:
                tile(i)
            tile(TILES - 1, last=True)
            square2(TILES - 1, evac_no(2, TILES - 1, True))
            square_root(evac_no(2, TILES - 1, True))

        @block.vector
        def _(dve):
            def by_columns(ap):
                return ap.rearrange("p (b d) -> p b d", d=COLS)

            def over_columns(t):
                return t[:].unsqueeze(2).to_broadcast([128, TB, COLS])

            def scale(i, e):
                dve.wait_ge(turned, (i + 1) * PAIRS)
                wait(dve, ssq_ready, e)
                nc.vector.tensor_tensor(by_columns(sq[:]), by_columns(acc12[:]), over_columns(rinv[1]), ALU.mult
                                        ).then_inc(scaled_ready, 1)

            def square_sum(e):
                dve.wait_ge(sq_ready, e + 1)
                wait(dve, nrm_ready, e)
                nc.vector.tensor_reduce(ssq[:], by_columns(sq[:]), AX.X, ALU.add).then_inc(ssq_ready, 1)

            def norm_step(n, layer, e):
                if n == 0:
                    dve.wait_ge(root_ready, e + 1)
                else:
                    dve.wait_ge(chain, e * CHAIN + n)
                if n == 0:
                    ins = nc.vector.reciprocal(rroot[:], root[:])
                elif n == 1:
                    ins = nc.vector.tensor_tensor(quot[:], nrm[:], rroot[:], ALU.mult)
                elif n == 2:
                    ins = nc.vector.scalar_tensor_tensor(half[:], quot[:], -0.5, rroot[:], ALU.mult, ALU.mult)
                else:
                    ins = nc.vector.scalar_tensor_tensor(rinv[layer][:], half[:], 1.5, rroot[:], ALU.add, ALU.mult)
                ins.then_inc(chain, 1)

            def divide(i, e):
                dve.wait_ge(chain, (e + 1) * CHAIN)
                wait(dve, ph_ready[0], i)
                wait(dve, pl_ready[0], i)
                nc.vector.scalar_tensor_tensor(by_columns(prev0[:]), by_columns(acc0[:]), bias[:, 0:1],
                                               over_columns(rinv[0]), ALU.add, ALU.mult).then_inc(prev0_ready, 1)

            def low0(i):
                dve.wait_ge(ph_ready[0], i + 1)
                dve.wait_ge(prev0_ready, i + 1)
                nc.vector.tensor_tensor(pl[0][:], prev0[:], ph[0][:].bitcast(f32), ALU.subtract
                                        ).then_inc(pl_ready[0], 1)

            def low1(i, h):
                cols = slice(h * PAIR, (h + 1) * PAIR)
                dve.wait_ge(ph_ready[1], i * 2 + h + 1)
                nc.vector.tensor_tensor(pl[1][:, cols], u1[:, cols], ph[1][:, cols].bitcast(f32), ALU.subtract
                                        ).then_inc(pl_ready[1], 1)

            def column_sum(layer, i):
                if layer == 0:
                    dve.wait_ge(prev0_ready, i + 1)
                    wait(dve, out_stored[0], i * 16)
                    nc.vector.tensor_reduce(outb[:, 0, :], by_columns(prev0[:]), AX.X, ALU.add).then_inc(out_ready, 1)
                    return
                if layer == 1:
                    dve.wait_ge(u1_ready, i * 2 + 2)
                if layer == 2:
                    dve.wait_ge(u2_ready, i + 1)
                source = u1 if layer == 1 else u2
                nc.vector.tensor_reduce(usum[:], by_columns(source[:]), AX.X, ALU.add).then_inc(summed[layer], 1)

            def output(layer, i, e):
                dve.wait_ge(chain, (e + 1) * CHAIN)
                dve.wait_ge(summed[layer], i + 1)
                wait(dve, out_stored[layer], i * 16)
                nc.vector.tensor_tensor(outb[:, layer, :], usum[:], rinv[layer][:], ALU.mult).then_inc(out_ready, 1)

            nc.vector.memset(w0t[0:FIELDS, 0, :], 0.0).then_inc(w0t_zeroed, 1)
            dve.wait_ge(w0_loaded, 80)
            p = PER_K * FIELDS
            nc.vector.tensor_tensor(w0s[0:p, 0:K0 - 1, :], w0s[0:p, 0:K0 - 1, :], w0t[0:p, 0:K0 - 1, :],
                                    ALU.add).then_inc(w0_summed, 1)
            nc.vector.tensor_tensor(w0s[0:LAST_K0, K0 - 1, :], w0s[0:LAST_K0, K0 - 1, :],
                                    w0t[0:LAST_K0, K0 - 1, :], ALU.add).then_inc(w0_summed, 1)
            dve.wait_ge(x0_loaded, X0_DMAS)
            for j in Z0_DVE_AT.values():
                product0(nc.vector, DVE, j)

            def low_weights(k, n):
                dve.wait_ge(wh_ready, k * len(PARTS) + n + 1)
                a, b = PARTS[n]
                nc.vector.tensor_tensor(wl[:, k, a:b, :], ws[:, k, a:b, :], wh[:, k, a:b, :].bitcast(f32),
                                        ALU.subtract).then_inc(wl_ready, 1)

            for n in range(len(PARTS)):
                low_weights(0, n)
            square_sum(0)
            for n in range(CHAIN):
                norm_step(n, 0, 0)
            divide(0, 0)
            column_sum(0, 0)
            low0(0)

            def multiply_add(i, v, m):
                layer, h = 1 + v // 2, v % 2
                g, t = divmod(m, GROUP)
                if m == h == 0:
                    dve.wait_ge(xrow_loaded[layer - 1], (i + 1) * 16)
                if t == 0:
                    dve.wait_ge(inner_ready[DVE], (i * PAIRS + v) * GROUPS + g + 1)
                source = inner[DVE][EVEN_SLOT[v * GROUPS + g]][:, t * UNITS:(t + 1) * UNITS]
                scalar = xrow[layer - 1][:, 2 * h, m:m + 1]
                sum_ = part[:, m % 2, :]
                if m < 2:
                    wait(dve, total_ready[DVE], i * PAIRS + v)
                    ins = nc.vector.tensor_scalar(sum_, source, scalar, None, ALU.mult)
                else:
                    dve.wait_ge(macs, mac_no(i, v, m) - 1)
                    ins = nc.vector.scalar_tensor_tensor(sum_, source, scalar, sum_, ALU.mult, ALU.add)
                ins.then_inc(macs, 1)

            def add_parts(i, v):
                dve.wait_ge(macs, mac_no(i, v + 1, 0))
                wait(dve, turned, i * PAIRS + v)
                nc.vector.tensor_tensor(total[DVE][:], part[:, 0, :], part[:, 1, :], ALU.add
                                        ).then_inc(total_ready[DVE], 1)

            def tile(i, first=False, last=False):
                after = [(2, i - 1, evac_no(2, i - 1))] if not first else []
                after += [(0, i + 1, evac_no(0, i + 1))] if not last else []
                after += [(1, i, evac_no(1, i, last))]

                def between(i, n):
                    if n in Z0_DVE_AT and not last:
                        dve.wait_ge(x0_loaded, (i + 2) * X0_DMAS)
                        product0(nc.vector, DVE, Z0_DVE_AT[n])
                    if first and n in LOW2_AT:
                        low_weights(1, LOW2_AT.index(n))
                    if n in LOW1_AT:
                        low1(i, LOW1_AT[n])
                    for layer, j, e in after:
                        if layer == 2 and n == SCALE_AT:
                            scale(j, e)
                        if n == SUM_AT[layer]:
                            square_sum(e)
                        if 0 <= n - CHAIN_AT[layer] < CHAIN:
                            norm_step(n - CHAIN_AT[layer], layer, e)
                        if layer == 0 and n == DIVIDE_AT:
                            divide(j, e)
                        if layer == 0 and n == LOW0_AT:
                            low0(j)
                        if n == COLUMNS_AT[layer]:
                            column_sum(layer, j)
                        if n == OUTPUT_AT.get(layer):
                            output(layer, j, e)

                for v in range(PAIRS):
                    for m in range(FIELDS):
                        multiply_add(i, v, m)
                        between(i, v * FIELDS + m)
                    add_parts(i, v)

            tile(0, first=True)
            with dve.Fori(1, TILES - 1) as i:
                tile(i)
            tile(TILES - 1, last=True)
            e = evac_no(2, TILES - 1, True)
            scale(TILES - 1, e)
            square_sum(e)
            column_sum(2, TILES - 1)
            for n in range(CHAIN):
                norm_step(n, 2, e)
            output(2, TILES - 1, e)

        @block.tensor
        def _(pe):
            def layer0(i, j):
                if j == 0:
                    wait(pe, prev0_ready, i)
                e = DVE if j in Z0_DVE_AT.values() else POOL
                mine = list((Z0_DVE_AT, Z0_POOL_AT)[e].values())
                pe.wait_ge(z0_ready[e], i * N_Z0[e] + mine.index(j) + 1)
                p = K0_PARTS[j]
                mm = nc.tensor.matmul(acc0[:], w0s[0:p, j, :], x0[0:p, j, :], start=j == 0, stop=j == K0 - 1)
                if j == K0 - 1:
                    mm.then_inc(acc0_ready, 1)

            def feature_sum(e):
                pe.wait_ge(ssq_ready, e + 1)
                wait(pe, chain, e * CHAIN)
                nc.tensor.matmul(nrm[:], ones[:], ssq[:], start=True, stop=True).then_inc(nrm_ready, 1)

            def turn(i, v):
                layer, h = 1 + v // 2, v % 2
                if layer == 1:
                    wait(pe, scaled_ready, i)
                else:
                    pe.wait_ge(ph_ready[1], i * 2 + h + 1)
                for e in (DVE, POOL):
                    pe.wait_ge(total_ready[e], i * PAIRS + v + 1)
                    chunk = 2 * h + e
                    mm = nc.tensor.transpose(acc12[:, chunk * 128:(chunk + 1) * 128], total[e][:], identity[:])
                mm.then_inc(turned, 1)

            def inner_sums(i, v, g, first):
                layer, h = 1 + v // 2, v % 2
                k, a, w = layer - 1, g * GROUP, WIDTH[g]
                if g == 0:
                    n = i + 1 if layer == 1 else i * 2 + h + 1
                    pe.wait_ge(ph_ready[k], n)
                    pe.wait_ge(pl_ready[k], n)
                if first and h == 0:
                    pe.wait_ge(wl_ready, k * len(PARTS) + PART_OF[a + w - 1] + 1)
                high = wh[:, k, a:a + w, :].rearrange("p m o -> p (m o)")
                low = wl[:, k, a:a + w, :].rearrange("p m o -> p (m o)")
                for e in (DVE, POOL):
                    rows = slice((2 * h + e) * 128, (2 * h + e + 1) * 128)
                    n = v * GROUPS + g
                    slot = (EVEN_SLOT[n], n % ODD_SLOTS)[e]
                    to = inner[e][slot][:, 0:w * UNITS]
                    if e == DVE:
                        wait(pe, macs, macs_by(i, max(
                            m for m in range(-EVEN_SLOTS - 1, n) if EVEN_SLOT[m] == slot)))
                    else:
                        wait(pe, products_ready, i * PAIRS * GROUPS + n - ODD_SLOTS + 1)
                    nc.tensor.matmul(to, ph[k][:, rows], high, start=True, stop=False)
                    nc.tensor.matmul(to, ph[k][:, rows], low, start=False, stop=False)
                    nc.tensor.matmul(to, pl[k][:, rows], high, start=False, stop=True).then_inc(inner_ready[e], 1)

            def tile(i, first=False, last=False):
                for v in range(PAIRS):
                    for g in range(GROUPS):
                        n = v * GROUPS + g
                        inner_sums(i, v, g, first)
                        if g == TURN_AT and v > 0:
                            turn(i, v - 1)
                        if g == TURN_AT and v == 0 and not first:
                            turn(i - 1, PAIRS - 1)
                        if n == FEATURES_AT[2] and not first:
                            feature_sum(evac_no(2, i - 1))
                        if n == FEATURES_AT[0] and not last:
                            feature_sum(evac_no(0, i + 1))
                        if n == FEATURES_AT[1]:
                            feature_sum(evac_no(1, i, last))
                        if n in LAYER0_AT and not last:
                            layer0(i + 1, LAYER0_AT.index(n))

            pe.wait_ge(ones_set, 1)
            pe.wait_ge(w0_summed, 2)
            for j in range(K0):
                layer0(0, j)
            feature_sum(0)
            pe.wait_ge(identity_loaded, 16)
            tile(0, first=True)
            with pe.Fori(1, TILES - 1) as i:
                tile(i)
            tile(TILES - 1, last=True)
            turn(TILES - 1, PAIRS - 1)
            feature_sum(evac_no(2, TILES - 1, True))


def kernel(r_x, L0_rec_w0, L0_rec_w1, L0_rec_w2, L0_rec_b0, L0_rec_b1, L0_rec_b2):
    import numpy as np
    import concourse.bacc as bacc
    from concourse.bass_utils import run_bass_kernel_spmd

    xt = np.asarray(r_x).transpose(1, 0, 2).reshape(FIELDS, BATCH * COLS)
    h = np.arange(FIELDS)[None, :]
    shifted = (h + np.arange(SHIFTS)[:, None]) % FIELDS
    w0 = np.asarray(L0_rec_w0).reshape(FIELDS, FIELDS, UNITS)
    arrays = {
        "x2": np.concatenate([xt, xt], axis=0),
        "xr": xt.reshape(FIELDS, TILES, CHUNKS, 128).transpose(1, 3, 2, 0),
        "eye": np.eye(128, dtype=xt.dtype),
        "w0a": w0[h, shifted],
        "w0b": w0[shifted, h],
        "w1": np.asarray(L0_rec_w1).reshape(FIELDS, UNITS, UNITS).transpose(1, 0, 2),
        "w2": np.asarray(L0_rec_w2).reshape(FIELDS, UNITS, UNITS).transpose(1, 0, 2),
        "b0": np.asarray(L0_rec_b0),
        "b1": np.asarray(L0_rec_b1),
        "b2": np.asarray(L0_rec_b2),
    }
    arrays = {k: np.ascontiguousarray(v) for k, v in arrays.items()}
    nc = bacc.Bacc("TRN2", target_bir_lowering=False, num_devices=1)
    args = [nc.dram_tensor(k, v.shape, mybir.dt.from_np(v.dtype), kind="ExternalInput").ap()
            for k, v in arrays.items()]
    out = nc.dram_tensor("out", (3, TILES, 128, TB), mybir.dt.float32, kind="ExternalOutput").ap()
    cin(nc, *args, out)
    r = run_bass_kernel_spmd(nc, [arrays], core_ids=[0])
    got = r.results[0]["out"]
    return got.transpose(1, 3, 0, 2).reshape(BATCH, 3 * UNITS)
```
